# Optimizing a Trainium2 kernel written in Bass

```python
import numpy as np
import jax
import jax.numpy as jnp

def _softmax(x, axis=-1):
    return jax.nn.softmax(x, axis=axis)

def _gelu(x):
    return jax.nn.gelu(x, approximate=True)

def _silu(x):
    return jax.nn.silu(x)

def _sigmoid(x):
    return jax.nn.sigmoid(x)

def _layernorm(x, axis=-1, eps=1e-05):
    m = jnp.mean(x, axis=axis, keepdims=True)
    v = jnp.var(x, axis=axis, keepdims=True)
    return (x - m) / jnp.sqrt(v + eps)

def _scatter_add(tgt, idx, src, axis=0):
    return tgt.at[idx].add(src)

def _segment_sum(src, seg, n):
    return jax.ops.segment_sum(src, seg, n)
kernel_name = 'mk_dlrm_tower_d1_rec_r8_315771'

def setup_inputs(seed: int=0):
    np.random.seed(seed)
    _w = jnp.asarray

    def _rec_inputs():
        import jax
        import jax.numpy as jnp
        _tk = jax.random.key(seed)
        ids = jnp.stack([jax.random.randint(jax.random.fold_in(_tk, 200 + f), (512,), 0, v, jnp.int32) for f, v in enumerate([12500, 1250, 125000, 12500, 12500, 1250, 1000, 1000, 12500, 1000, 12500, 1250, 12500, 1250, 1000, 12500, 1000, 1000, 1000, 1250, 1250, 12500, 1250, 1250, 1250, 1250])], axis=1)
        tbl_0 = 0.05 * jax.random.normal(jax.random.fold_in(_tk, 500 + 0), (12500, 128), jnp.float32)
        tbl_1 = 0.05 * jax.random.normal(jax.random.fold_in(_tk, 500 + 1), (1250, 128), jnp.float32)
        tbl_2 = 0.05 * jax.random.normal(jax.random.fold_in(_tk, 500 + 2), (125000, 128), jnp.float32)
        tbl_3 = 0.05 * jax.random.normal(jax.random.fold_in(_tk, 500 + 3), (12500, 128), jnp.float32)
        tbl_4 = 0.05 * jax.random.normal(jax.random.fold_in(_tk, 500 + 4), (12500, 128), jnp.float32)
        tbl_5 = 0.05 * jax.random.normal(jax.random.fold_in(_tk, 500 + 5), (1250, 128), jnp.float32)
        tbl_6 = 0.05 * jax.random.normal(jax.random.fold_in(_tk, 500 + 6), (1000, 128), jnp.float32)
        tbl_7 = 0.05 * jax.random.normal(jax.random.fold_in(_tk, 500 + 7), (1000, 128), jnp.float32)
        tbl_8 = 0.05 * jax.random.normal(jax.random.fold_in(_tk, 500 + 8), (12500, 128), jnp.float32)
        tbl_9 = 0.05 * jax.random.normal(jax.random.fold_in(_tk, 500 + 9), (1000, 128), jnp.float32)
        tbl_10 = 0.05 * jax.random.normal(jax.random.fold_in(_tk, 500 + 10), (12500, 128), jnp.float32)
        tbl_11 = 0.05 * jax.random.normal(jax.random.fold_in(_tk, 500 + 11), (1250, 128), jnp.float32)
        tbl_12 = 0.05 * jax.random.normal(jax.random.fold_in(_tk, 500 + 12), (12500, 128), jnp.float32)
        tbl_13 = 0.05 * jax.random.normal(jax.random.fold_in(_tk, 500 + 13), (1250, 128), jnp.float32)
        tbl_14 = 0.05 * jax.random.normal(jax.random.fold_in(_tk, 500 + 14), (1000, 128), jnp.float32)
        tbl_15 = 0.05 * jax.random.normal(jax.random.fold_in(_tk, 500 + 15), (12500, 128), jnp.float32)
        tbl_16 = 0.05 * jax.random.normal(jax.random.fold_in(_tk, 500 + 16), (1000, 128), jnp.float32)
        tbl_17 = 0.05 * jax.random.normal(jax.random.fold_in(_tk, 500 + 17), (1000, 128), jnp.float32)
        tbl_18 = 0.05 * jax.random.normal(jax.random.fold_in(_tk, 500 + 18), (1000, 128), jnp.float32)
        tbl_19 = 0.05 * jax.random.normal(jax.random.fold_in(_tk, 500 + 19), (1250, 128), jnp.float32)
        tbl_20 = 0.05 * jax.random.normal(jax.random.fold_in(_tk, 500 + 20), (1250, 128), jnp.float32)
        tbl_21 = 0.05 * jax.random.normal(jax.random.fold_in(_tk, 500 + 21), (12500, 128), jnp.float32)
        tbl_22 = 0.05 * jax.random.normal(jax.random.fold_in(_tk, 500 + 22), (1250, 128), jnp.float32)
        tbl_23 = 0.05 * jax.random.normal(jax.random.fold_in(_tk, 500 + 23), (1250, 128), jnp.float32)
        tbl_24 = 0.05 * jax.random.normal(jax.random.fold_in(_tk, 500 + 24), (1250, 128), jnp.float32)
        tbl_25 = 0.05 * jax.random.normal(jax.random.fold_in(_tk, 500 + 25), (1250, 128), jnp.float32)
        _rk = jax.random.fold_in(_tk, 7)
        r_dense_features = 7.22013e-05 + 1.00017 * jax.random.normal(jax.random.fold_in(_rk, 101), (512, 128), jnp.float32)
        W_top1 = 0.0456912 * jax.random.normal(jax.random.fold_in(_tk, 801), (479, 512), jnp.float32)
        W_top2 = 0.0441942 * jax.random.normal(jax.random.fold_in(_tk, 802), (512, 256), jnp.float32)
        W_top3 = 0.0625 * jax.random.normal(jax.random.fold_in(_tk, 803), (256, 1), jnp.float32)
        b_top1 = jnp.zeros((512,), jnp.float32)
        b_top2 = jnp.zeros((256,), jnp.float32)
        return (r_dense_features, ids, tbl_0, tbl_1, tbl_2, tbl_3, tbl_4, tbl_5, tbl_6, tbl_7, tbl_8, tbl_9, tbl_10, tbl_11, tbl_12, tbl_13, tbl_14, tbl_15, tbl_16, tbl_17, tbl_18, tbl_19, tbl_20, tbl_21, tbl_22, tbl_23, tbl_24, tbl_25, W_top1, b_top1, W_top2, b_top2, W_top3)
    r_dense_features, ids, tbl_0, tbl_1, tbl_2, tbl_3, tbl_4, tbl_5, tbl_6, tbl_7, tbl_8, tbl_9, tbl_10, tbl_11, tbl_12, tbl_13, tbl_14, tbl_15, tbl_16, tbl_17, tbl_18, tbl_19, tbl_20, tbl_21, tbl_22, tbl_23, tbl_24, tbl_25, W_top1, b_top1, W_top2, b_top2, W_top3 = _rec_inputs()

    def _L0_rec_setup():
        import jax, jax.numpy as jnp
        import numpy as np
        FEATURE_NUM = 27
        key = jax.random.key(seed)
        k1, k2 = jax.random.split(key)
        B, N, D = (8192, FEATURE_NUM - 1, 128)
        dense_features = jax.random.normal(k1, (B, D), dtype=jnp.float32)
        sparse_features = jax.random.normal(k2, (B, N, D), dtype=jnp.float32)
        return {'dense_features': dense_features, 'sparse_features': sparse_features}
    _L0_rec_all = _L0_rec_setup()
    _L0_rec_in = {k: v for k, v in _L0_rec_all.items() if k in ()}
    del _L0_rec_all
    return {'r_dense_features': r_dense_features, 'ids': ids, 'tbl_0': tbl_0, 'tbl_1': tbl_1, 'tbl_2': tbl_2, 'tbl_3': tbl_3, 'tbl_4': tbl_4, 'tbl_5': tbl_5, 'tbl_6': tbl_6, 'tbl_7': tbl_7, 'tbl_8': tbl_8, 'tbl_9': tbl_9, 'tbl_10': tbl_10, 'tbl_11': tbl_11, 'tbl_12': tbl_12, 'tbl_13': tbl_13, 'tbl_14': tbl_14, 'tbl_15': tbl_15, 'tbl_16': tbl_16, 'tbl_17': tbl_17, 'tbl_18': tbl_18, 'tbl_19': tbl_19, 'tbl_20': tbl_20, 'tbl_21': tbl_21, 'tbl_22': tbl_22, 'tbl_23': tbl_23, 'tbl_24': tbl_24, 'tbl_25': tbl_25, 'W_top1': W_top1, 'b_top1': b_top1, 'W_top2': W_top2, 'b_top2': b_top2, 'W_top3': W_top3}

def reference(r_dense_features, ids, tbl_0, tbl_1, tbl_2, tbl_3, tbl_4, tbl_5, tbl_6, tbl_7, tbl_8, tbl_9, tbl_10, tbl_11, tbl_12, tbl_13, tbl_14, tbl_15, tbl_16, tbl_17, tbl_18, tbl_19, tbl_20, tbl_21, tbl_22, tbl_23, tbl_24, tbl_25, W_top1, b_top1, W_top2, b_top2, W_top3):
    import jax
    import jax.numpy as jnp

    def _L0_rec_ref(dense_features, sparse_features):
        import jax, jax.numpy as jnp
        import numpy as np
        FEATURE_NUM = 27
        combined = jnp.concatenate([dense_features[:, None, :], sparse_features], axis=1)
        interactions = jnp.einsum('bfd,bgd->bfg', combined, combined)
        iu, ju = jnp.triu_indices(FEATURE_NUM, k=1)
        return interactions[:, iu, ju]
    e = jnp.stack([tbl_0[ids[:, 0]], tbl_1[ids[:, 1]], tbl_2[ids[:, 2]], tbl_3[ids[:, 3]], tbl_4[ids[:, 4]], tbl_5[ids[:, 5]], tbl_6[ids[:, 6]], tbl_7[ids[:, 7]], tbl_8[ids[:, 8]], tbl_9[ids[:, 9]], tbl_10[ids[:, 10]], tbl_11[ids[:, 11]], tbl_12[ids[:, 12]], tbl_13[ids[:, 13]], tbl_14[ids[:, 14]], tbl_15[ids[:, 15]], tbl_16[ids[:, 16]], tbl_17[ids[:, 17]], tbl_18[ids[:, 18]], tbl_19[ids[:, 19]], tbl_20[ids[:, 20]], tbl_21[ids[:, 21]], tbl_22[ids[:, 22]], tbl_23[ids[:, 23]], tbl_24[ids[:, 24]], tbl_25[ids[:, 25]]], axis=1)
    z = _L0_rec_ref(r_dense_features, e)
    z = z.reshape(z.shape[0], -1)
    h = jnp.concatenate([z, r_dense_features], axis=1)
    h = jnp.maximum(h @ W_top1 + b_top1, 0.0)
    h = jnp.maximum(h @ W_top2 + b_top2, 0.0)
    y = h @ W_top3
    return y

_drawn_inputs = setup_inputs


def setup_inputs(seed=0):
    import zlib

    import numpy as np

    out = dict(_drawn_inputs(seed))
    spreads = {'b_top1': (0.0, 0.1), 'b_top2': (0.0, 0.1)}
    factors = {}
    for name, (base, spread) in spreads.items():
        noise = np.random.default_rng([zlib.crc32(name.encode()), seed]).standard_normal(out[name].shape)
        drawn = base * np.exp(spread * noise) if base else spread * noise
        out[name] = jnp.asarray(drawn.astype(out[name].dtype))
    for name, factor in factors.items():
        out[name] = (out[name] * factor).astype(out[name].dtype)
    return out
```

```python
import concourse.bass as bass
from concourse import mybir
from contextlib import ExitStack


def dlrm_tower(nc, ids, dense, tables, w1_pairs, w1_dense, b1, w2, b2, w3, out):
    fp32 = mybir.dt.float32
    ALU = mybir.AluOpType
    ACT = mybir.ActivationFunctionType

    P = 128
    BATCH = out.shape[1]
    TILES = BATCH // P
    D = dense.shape[1]
    NT = len(tables)
    NF = NT + 1
    QUAD = 4
    NQ = -(-NF // QUAD)
    SHIFTS = NF // 2
    PITCH = NF + SHIFTS
    KI = 9
    KP = NF // KI
    H1, H2 = w1_dense.shape[1], w2.shape[1]
    M1, M2 = H1 // P, H2 // P
    BLK = 32
    QUADRANTS = P // BLK

    def quad_features(q):
        return range(QUAD * q, min(QUAD * q + QUAD, NF))

    def quad_samples_sem(q):
        return 16 * sum(1 for f in quad_features(q) if f > 0)

    ctx = ExitStack()
    with ctx:
        def sb(name, shape, dt=fp32):
            return ctx.enter_context(nc.sbuf_tensor(name, shape, dt))

        def ps(name, shape):
            return ctx.enter_context(nc.psum_tensor(name, shape, fp32))

        def sem(name):
            return ctx.enter_context(nc.semaphore(name))

        ids_sb = sb("ids_sb", [P, TILES, NT], mybir.dt.int32)
        emb = sb("emb", [P, TILES, NF, D])
        identity = sb("identity", [P, P])
        feat_t = sb("feat_t", [P, TILES, P * NF + BLK - NF])
        feat_v = feat_t[:, :, 0:P * NF].rearrange("p t (b f) -> p t b f", f=NF)
        pairs = sb("pairs", [P, BLK * PITCH])
        packed = sb("packed", [P, 2, NF * SHIFTS])
        pairs_t = sb("pairs_t", [KI * SHIFTS, TILES, KP, P])
        h1_t = sb("h1_t", [P, TILES, M1, P])
        h2_t = sb("h2_t", [P, TILES, M2, P])
        y_row = sb("y_row", [1, BATCH])
        w1p_sb = sb("w1p_sb", [KI * SHIFTS, KP, H1])
        w1d_sb = sb("w1d_sb", [P, H1])
        w2_sb = sb("w2_sb", [P, M1, H2])
        w3_sb = sb("w3_sb", [P, M2])
        b1_sb = sb("b1_sb", [P, M1])
        b2_sb = sb("b2_sb", [P, M2])

        tr_ps = [ps(f"tr_ps{i}", [P, QUAD, P]) for i in range(2)]
        gram_ps = ps("gram_ps", [P, BLK, BLK])
        h1_ps = [ps(f"h1_ps{i}", [P, QUAD, P]) for i in range(2)]
        y_bank = ps("y_bank", [P, QUAD, P])
        pairs_t_ps = ps("pairs_t_ps", [P, QUAD, P])
        h2_ps = [y_bank[:, 0, :], pairs_t_ps[:, QUAD - 1, :]]
        y_ps = y_bank[0:1, 1, :]

        ids_in = sem("ids_in")
        dense_in = sem("dense_in")
        weights_in = sem("weights_in")
        identity_zero = sem("identity_zero")
        identity_ready = sem("identity_ready")
        tail_zero = sem("tail_zero")
        gathered = [[sem(f"gathered_{t}_{q}") for q in range(NQ)] for t in range(TILES)]
        quad_transposed = sem("quad_transposed")
        quad_copied = [sem("quad_copied_dve"), sem("quad_copied_act")]
        gram_ready = sem("gram_ready")
        pairs_ready = sem("pairs_ready")
        packed_ready = sem("packed_ready")
        pairs_transposed = sem("pairs_transposed")
        pairs_t_ready = sem("pairs_t_ready")
        h1_summed = sem("h1_summed")
        h1_ready = [sem("h1_ready_dve"), sem("h1_ready_act")]
        h2_summed = sem("h2_summed")
        h2_ready = [sem("h2_ready_dve"), sem("h2_ready_act")]
        y_summed = sem("y_summed")
        y_ready = sem("y_ready")
        y_out = sem("y_out")

        block = ctx.enter_context(nc.Block())

        @block.sync
        def _(sp):
            sp.dma_start(ids_sb[:], ids).then_inc(ids_in, 16)
            sp.dma_start(emb[:, :, 0, :], dense.rearrange("(t p) d -> p t d", p=P)).then_inc(dense_in, 16)
            for dst, src in ((w1p_sb[:], w1_pairs), (w1d_sb[:], w1_dense),
                             (w2_sb[:], w2.rearrange("(k p) n -> p k n", p=P)),
                             (b1_sb[:], b1), (b2_sb[:], b2), (w3_sb[:], w3)):
                sp.dma_start(dst, src).then_inc(weights_in, 16)
            sp.wait_ge(y_ready, TILES)
            sp.dma_start(out, y_row[:]).then_inc(y_out, 16)
            sp.wait_ge(y_out, 16)

        @block.gpsimd
        def _(pool):
            nc.gpsimd.memset(feat_t[:, :, P * NF:], 0.0).then_inc(tail_zero, 1)
            nc.gpsimd.memset(identity[:], 0.0).then_inc(identity_zero, 1)
            pool.wait_ge(identity_zero, 1)
            nc.gpsimd.affine_select(out=identity[:], in_=identity[:], compare_op=ALU.not_equal, fill=1.0,
                                    base=0, pattern=[[-1, P]], channel_multiplier=1).then_inc(identity_ready, 1)
            pool.wait_ge(ids_in, 16)
            for t in range(TILES):
                for q in range(NQ):
                    for f in quad_features(q):
                        if f > 0:
                            pool.indirect_dma_start(
                                emb[:, t, f, :], None, tables[f - 1],
                                bass.IndirectOffsetOnAxis(ap=ids_sb[:, t, f - 1:f], axis=0),
                            ).then_inc(gathered[t][q], 16)

        def copy_quad(eng, copy, n):
            t, q = divmod(n, NQ)
            fs = quad_features(q)
            eng.wait_ge(quad_transposed, n + 1)
            copy(feat_v[:, t, :, fs[0]:fs[-1] + 1].rearrange("p b f -> p f b"),
                 tr_ps[n % 2][:, 0:len(fs), :]).then_inc(quad_copied[n % 2], 1)

        @block.vector
        def _(dve):
            def mlp_steps(t):
                dve.wait_ge(pairs_transposed, t + 1)
                nc.vector.tensor_copy(pairs_t[:, t, :, :], pairs_t_ps[0:KI * SHIFTS, 0:KP, :]).then_inc(
                    pairs_t_ready, 1)
                for m in range(0, M1, 2):
                    if t == 0 and m == 0:
                        dve.wait_ge(weights_in, 96)
                    dve.wait_ge(h1_summed, M1 * t + m + 1)
                    nc.vector.tensor_scalar(h1_t[:, t, m, :], h1_ps[m % 2][:, m // 2, :], b1_sb[:, m:m + 1], 0.0,
                                            ALU.add, ALU.max).then_inc(h1_ready[0], 1)
                dve.wait_ge(h2_summed, M2 * t + 1)
                nc.vector.tensor_scalar(h2_t[:, t, 0, :], h2_ps[0], b2_sb[:, 0:1], 0.0,
                                        ALU.add, ALU.max).then_inc(h2_ready[0], 1)
                dve.wait_ge(y_summed, t + 1)
                nc.vector.tensor_copy(y_row[:, t * P:(t + 1) * P], y_ps).then_inc(y_ready, 1)

            for t in range(TILES):
                for n in range(t * NQ, (t + 1) * NQ):
                    if n % 2 == 0:
                        copy_quad(dve, nc.vector.tensor_copy, n)
                dve.wait_ge(gram_ready, t + 1)
                if t >= 1:
                    dve.wait_ge(packed_ready, t)
                by_j = gram_ps[:].rearrange("p g j -> p j g")
                to_j = pairs[:].rearrange("p (i j) -> p j i", j=PITCH)
                nc.vector.transpose(to_j[:, 1:NF, :], by_j[:, 1:NF, :])
                nc.vector.transpose(to_j[:, NF:PITCH, :], by_j[:, 0:SHIFTS, :]).then_inc(pairs_ready, 1)
                dve.wait_ge(pairs_ready, t + 1)
                if t >= 2:
                    dve.wait_ge(pairs_transposed, t - 1)
                rows = pairs[:, 1:1 + NF * (PITCH + 1)].rearrange("p (i s) -> p i s", i=NF)
                nc.vector.tensor_copy(packed[:, t % 2, :].rearrange("p (i s) -> p i s", i=NF),
                                      rows[:, :, 0:SHIFTS]).then_inc(packed_ready, 1)
                mlp_steps(t)

        @block.scalar
        def _(act):
            act.wait_ge(weights_in, 96)
            for t in range(TILES):
                for n in range(t * NQ, (t + 1) * NQ):
                    if n % 2 == 1:
                        copy_quad(act, nc.scalar.copy, n)
                for m in range(1, M1, 2):
                    act.wait_ge(h1_summed, M1 * t + m + 1)
                    nc.scalar.activation(h1_t[:, t, m, :], h1_ps[m % 2][:, m // 2, :], ACT.Relu,
                                         bias=b1_sb[:, m:m + 1]).then_inc(h1_ready[1], 1)
                act.wait_ge(h2_summed, M2 * t + 2)
                nc.scalar.activation(h2_t[:, t, 1, :], h2_ps[1], ACT.Relu,
                                     bias=b2_sb[:, 1:2]).then_inc(h2_ready[1], 1)

        @block.tensor
        def _(pe):
            pe.wait_ge(identity_ready, 1)
            pe.wait_ge(dense_in, 16)
            pe.wait_ge(tail_zero, 1)
            for t in range(TILES):
                for n in range(t * NQ, (t + 1) * NQ):
                    q = n - t * NQ
                    pe.wait_ge(gathered[t][q], quad_samples_sem(q))
                    if n >= 2:
                        pe.wait_ge(quad_copied[n % 2], n // 2)
                    for k, f in enumerate(quad_features(q)):
                        last = nc.tensor.transpose(tr_ps[n % 2][:, k, :], emb[:, t, f, :], identity[:])
                    last.then_inc(quad_transposed, 1)
                n = (t + 1) * NQ
                pe.wait_ge(quad_copied[0], (n + 1) // 2)
                pe.wait_ge(quad_copied[1], n // 2)
                if t >= 1:
                    pe.wait_ge(pairs_ready, t)
                for g in range(BLK):
                    for c in range(QUADRANTS):
                        at = (BLK * c + g) * NF
                        last = nc.tensor.matmul(gram_ps[BLK * c:BLK * (c + 1), g, 0:NF],
                                                feat_t[:, t, at:at + BLK], feat_t[:, t, at:at + NF],
                                                start=True, stop=True)
                last.then_inc(gram_ready, 1)

                pe.wait_ge(packed_ready, t + 1)
                if t >= 1:
                    pe.wait_ge(h2_ready[1], t)
                for k in range(KP):
                    last = nc.tensor.transpose(pairs_t_ps[0:KI * SHIFTS, k, :],
                                               packed[:, t % 2, KI * SHIFTS * k:KI * SHIFTS * (k + 1)],
                                               identity[:])
                last.then_inc(pairs_transposed, 1)

                if t == 0:
                    pe.wait_ge(weights_in, 96)
                pe.wait_ge(pairs_t_ready, t + 1)
                for m in range(M1):
                    if t >= 1 or m >= 2:
                        pe.wait_ge(h1_ready[m % 2], (M1 // 2) * t + m // 2)
                    units = slice(m * P, (m + 1) * P)
                    nc.tensor.matmul(h1_ps[m % 2][:, m // 2, :], w1d_sb[:, units], feat_v[:, t, :, 0],
                                     start=True, stop=False)
                    for k in range(KP):
                        last = nc.tensor.matmul(h1_ps[m % 2][:, m // 2, :], w1p_sb[:, k, units], pairs_t[:, t, k, :],
                                                start=False, stop=(k == KP - 1))
                    last.then_inc(h1_summed, 1)
                for m in range(M2):
                    if t >= 1 and m == 0:
                        pe.wait_ge(y_ready, t)
                    for k in range(M1):
                        if m == 0:
                            pe.wait_ge(h1_ready[k % 2], (M1 // 2) * t + k // 2 + 1)
                        last = nc.tensor.matmul(h2_ps[m], w2_sb[:, k, m * P:(m + 1) * P], h1_t[:, t, k, :],
                                                start=(k == 0), stop=(k == M1 - 1))
                    last.then_inc(h2_summed, 1)
                for k in range(M2):
                    pe.wait_ge(h2_ready[k], t + 1)
                    last = nc.tensor.matmul(y_ps, w3_sb[:, k:k + 1], h2_t[:, t, k, :],
                                            start=(k == 0), stop=(k == M2 - 1))
                last.then_inc(y_summed, 1)


_TABLES = 26
_FEATURES = _TABLES + 1


def _pair_rows():
    import numpy as _np

    row = {}
    for a in range(_FEATURES):
        for b in range(a + 1, _FEATURES):
            row[a, b] = len(row)
    rows = [row[min(i, (i + s) % _FEATURES), max(i, (i + s) % _FEATURES)]
            for i in range(_FEATURES) for s in range(1, _FEATURES // 2 + 1)]
    return _np.array(rows)


def kernel(**inputs):
    import numpy as _np
    import concourse.bacc as _bacc
    from concourse import mybir as _mybir
    from concourse.bass_utils import run_bass_kernel_spmd as _run

    ids = _np.asarray(inputs["ids"])
    w1 = _np.asarray(inputs["W_top1"])
    batch = ids.shape[0]
    rows = _pair_rows()
    laid_out = {
        "ids": ids.reshape(batch // 128, 128, _TABLES).transpose(1, 0, 2),
        "dense": _np.asarray(inputs["r_dense_features"]),
        "w1_pairs": w1[rows].reshape(3, len(rows) // 3, -1).transpose(1, 0, 2),
        "w1_dense": w1[len(rows):],
        "b1": _np.asarray(inputs["b_top1"]).reshape(-1, 128).T,
        "w2": _np.asarray(inputs["W_top2"]),
        "b2": _np.asarray(inputs["b_top2"]).reshape(-1, 128).T,
        "w3": _np.asarray(inputs["W_top3"]).reshape(-1, 128).T,
    }
    for f in range(_TABLES):
        laid_out[f"tbl_{f}"] = _np.asarray(inputs[f"tbl_{f}"])

    nc = _bacc.Bacc("TRN2", target_bir_lowering=False, num_devices=1)
    arrays, aps = {}, {}
    for name, a in laid_out.items():
        a = _np.ascontiguousarray(a)
        arrays[f"in_{name}_dram"] = a
        aps[name] = nc.dram_tensor(f"in_{name}_dram", a.shape, _mybir.dt.from_np(a.dtype),
                                   kind="ExternalInput").ap()
    out = nc.dram_tensor("out_dram", (1, batch), _mybir.dt.float32, kind="ExternalOutput").ap()
    dlrm_tower(nc, aps["ids"], aps["dense"], [aps[f"tbl_{f}"] for f in range(_TABLES)],
               aps["w1_pairs"], aps["w1_dense"], aps["b1"], aps["w2"], aps["b2"], aps["w3"], out)
    r = _run(nc, [arrays], core_ids=[0])
    return r.results[0]["out_dram"].reshape(batch, 1)
```

```python
import concourse.bass as bass
from concourse import mybir
from contextlib import ExitStack


def dlrm_tower(nc, ids, picked_ids, dense, tables, w1_pairs, w1_dense, b1, w2, b2, w3, out):
    fp32 = mybir.dt.float32
    fp32r = mybir.dt.float32r
    int32 = mybir.dt.int32
    ALU = mybir.AluOpType
    ACT = mybir.ActivationFunctionType

    P = 128
    BATCH = out.shape[1]
    TILES = BATCH // P
    D = dense.shape[1]
    NT = len(tables)
    NF = NT + 1
    QUAD = 4
    NS = picked_ids.shape[0]
    TS = TILES - picked_ids.shape[1] // P
    picked_tables = tables[NT - NS:]
    TROWS = 125
    CHUNKS = [tbl.shape[0] // TROWS for tbl in picked_tables]
    KMAX = max(CHUNKS)
    SLOTS = 12
    LOADS = 3
    SHIFTS = NF // 2
    PITCH = NF + SHIFTS
    KI = 9
    KP = NF // KI
    H1, H2 = w1_dense.shape[1], w2.shape[1]
    M1, M2 = H1 // P, H2 // P
    BLK = 32
    QUADRANTS = P // BLK

    def quads(t):
        n = NF if t < TS else NF - NS
        return [range(f, min(f + QUAD, n)) for f in range(0, n, QUAD)]

    STEPS = {
        (0, "start"): [("select", 0)],
        (0, 1): [("select", 1)],
        (0, 2): [("select", 2)],
        (0, 3): [("select", 3)],
        (0, 4): [("select", 4)],
        (0, 6): [("select", 5)],
        (0, "gram"): [("select", 6), ("pairs", 0), ("dense", 0)],
        (1, 0): [("layer1", 0), ("select", 7)],
        (1, 1): [("select", 8)],
        (1, 4): [("layer2", 0)],
        (2, 0): [("layer3", 0)],
        (2, 1): [("pairs", 1), ("dense", 1)],
        (2, 2): [("layer1", 1)],
        (2, 4): [("layer2", 1)],
        (3, 0): [("layer3", 1)],
        (3, 1): [("pairs", 2), ("dense", 2)],
        (3, 2): [("layer1", 2)],
        (3, 4): [("layer2", 2)],
        (3, "gram"): [("dense", 3), ("warm", 7), ("pairs", 3), ("layer3", 2), ("layer1", 3), ("layer2", 3), ("layer3", 3)],
    }

    def steps_after(t, q):
        return STEPS.get((t, q), [])

    RING = 3
    turn = {}
    for t, q in [(0, "start")] + [(t, q) for t in range(TILES) for q in [*range(len(quads(t))), "gram"]]:
        if q in range(len(quads(t))):
            turn["quad", t, q] = len(turn)
        for step in steps_after(t, q):
            if step[0] in ("select", "layer3"):
                turn[step] = len(turn)

    ctx = ExitStack()
    with ctx:
        def sb(name, shape, dt=fp32):
            return ctx.enter_context(nc.sbuf_tensor(name, shape, dt))

        def ps(name, shape):
            return ctx.enter_context(nc.psum_tensor(name, shape, fp32))

        def sem(name):
            return ctx.enter_context(nc.semaphore(name))

        ids_sb = sb("ids_sb", [P, TILES, NT], mybir.dt.int32)
        dense_sb = sb("dense_sb", [P, TILES, D])
        emb = [sb(f"emb{t}", [P, quads(t)[-1][-1], D]) for t in range(TILES)]
        identity = sb("identity", [P, P])
        feat_t = sb("feat_t", [P, TILES, P * NF + BLK - NF])
        feat_v = feat_t[:, :, 0:P * NF].rearrange("p t (b f) -> p t b f", f=NF)
        pairs = sb("pairs", [P, BLK * PITCH])
        packed = sb("packed", [P, 2, NF * SHIFTS])
        pairs_t = sb("pairs_t", [KI * SHIFTS, KP, P])
        h1_t = sb("h1_t", [P, M1, P])
        h2_t = sb("h2_t", [P, TILES, M2, P])
        ids_all = sb("ids_all", [P, LOADS, (TILES - TS) * P], int32)
        row_int = [sb(f"row_int{k}", [TROWS, k], int32) for k in sorted(set(CHUNKS))]
        row_of = {k: sb(f"row_of{k}", [TROWS, k]) for k in sorted(set(CHUNKS))}
        table_raw = sb("table_raw", [TROWS, LOADS, KMAX * D])
        table_hi = sb("table_hi", [TROWS, 2, KMAX * D], fp32r)
        table_lo = sb("table_lo", [TROWS, 2, KMAX * D], fp32r)
        one_hot = sb("one_hot", [TROWS, SLOTS, (TILES - TS) * P], fp32r)
        y_row = sb("y_row", [1, BATCH])
        w1p_sb = sb("w1p_sb", [KI * SHIFTS, KP, H1])
        w1d_sb = sb("w1d_sb", [P, H1])
        w2_sb = sb("w2_sb", [P, M1, H2])
        w3_sb = sb("w3_sb", [P, M2])
        b1_sb = sb("b1_sb", [P, M1])
        b2_sb = sb("b2_sb", [P, M2])

        ring = [ps(f"ring{i}", [P, QUAD, P]) for i in range(RING)]
        gram_ps = ps("gram_ps", [P, BLK, BLK])
        pairs_t_ps = ps("pairs_t_ps", [P, QUAD, P])
        mlp_ps = [ps(f"mlp_ps{i}", [P, QUAD, P]) for i in range(2)]
        h1_ps = [mlp_ps[m % 2][:, m // 2, :] for m in range(M1)]
        h2_ps = [mlp_ps[0][:, M1 // 2, :], pairs_t_ps[:, KP, :]]

        ids_in = sem("ids_in")
        dense_in = sem("dense_in")
        weights_in = sem("weights_in")
        identity_zero = sem("identity_zero")
        identity_ready = sem("identity_ready")
        tail_zero = sem("tail_zero")
        gathered = [[sem(f"gathered_{t}_{q}") for q in range(len(quads(t)))] for t in range(TILES)]
        ring_filled = sem("ring_filled")
        ring_copied = sem("ring_copied")
        rows_numbered = sem("rows_numbered")
        row_of_ready = sem("row_of_ready")
        ids_all_in = [sem(f"ids_all_in{i}") for i in range(LOADS)]
        table_in = [sem(f"table_in{i}") for i in range(LOADS)]
        hi_ready = sem("hi_ready")
        lo_ready = sem("lo_ready")
        one_hot_ready = sem("one_hot_ready")
        one_hot_used = sem("one_hot_used")
        ids_all_used = sem("ids_all_used")
        gram_ready = sem("gram_ready")
        pairs_ready = sem("pairs_ready")
        packed_ready = sem("packed_ready")
        pairs_transposed = sem("pairs_transposed")
        pairs_t_ready = sem("pairs_t_ready")
        h1_summed = sem("h1_summed")
        h1_ready = [sem("h1_ready_dve"), sem("h1_ready_act")]
        h2_summed = sem("h2_summed")
        h2_ready = [sem("h2_ready_dve"), sem("h2_ready_act")]
        y_out = sem("y_out")

        block = ctx.enter_context(nc.Block())

        @block.sync
        def _(sp):
            sp.dma_start(ids_sb[:], ids).then_inc(ids_in, 16)

            def load_table(s):
                if s >= LOADS:
                    sp.wait_ge(ids_all_used, s - LOADS + 1)
                sp.dma_start(ids_all[:, s % LOADS, :],
                             picked_ids[s:s + 1, :].to_broadcast([P, picked_ids.shape[1]])).then_inc(
                                 ids_all_in[s % LOADS], 16)
                n = CHUNKS[s]
                rows = picked_tables[s].rearrange("(p k) d -> p (k d)", k=n)
                for a, b in ((0, 112), (112, TROWS)):
                    sp.dma_start(table_raw[a:b, s % LOADS, 0:n * D], rows[a:b, :]).then_inc(
                        table_in[s % LOADS], 16)

            load_table(0)
            sp.dma_start(dense_sb[:], dense.rearrange("(t p) d -> p t d", p=P)).then_inc(dense_in, 16)
            for s in range(1, NS):
                load_table(s)
                if s == LOADS:
                    for dst, src in ((w1p_sb[:], w1_pairs), (w1d_sb[:], w1_dense),
                                     (w2_sb[:], w2.rearrange("(k p) n -> p k n", p=P)),
                                     (b1_sb[:], b1), (b2_sb[:], b2), (w3_sb[:], w3)):
                        sp.dma_start(dst, src).then_inc(weights_in, 16)
            sp.wait_ge(ring_copied, len(turn))
            sp.dma_start(out, y_row[:]).then_inc(y_out, 16)
            sp.wait_ge(y_out, 16)

        @block.gpsimd
        def _(pool):
            nc.gpsimd.memset(feat_t[:, :, P * NF:], 0.0).then_inc(tail_zero, 1)
            nc.gpsimd.memset(identity[:], 0.0).then_inc(identity_zero, 1)
            for rows in row_int:
                nc.gpsimd.iota(rows[:], pattern=[[1, rows.shape[1]]], base=0,
                               channel_multiplier=rows.shape[1]).then_inc(rows_numbered, 1)
            pool.wait_ge(identity_zero, 1)
            nc.gpsimd.affine_select(out=identity[:], in_=identity[:], compare_op=ALU.not_equal, fill=1.0,
                                    base=0, pattern=[[-1, P]], channel_multiplier=1).then_inc(identity_ready, 1)
            pool.wait_ge(ids_in, 16)
            for t in range(TILES):
                for q, features in enumerate(quads(t)):
                    for f in features:
                        if f > 0:
                            pool.indirect_dma_start(
                                emb[t][:, f - 1, :], None, tables[f - 1],
                                bass.IndirectOffsetOnAxis(ap=ids_sb[:, t, f - 1:f], axis=0),
                            ).then_inc(gathered[t][q], 16)

        @block.vector
        def _(dve):
            def make_one_hot(s):
                n, before = CHUNKS[s], sum(CHUNKS[:s])
                dve.wait_ge(ids_all_in[s % LOADS], 16 * (s // LOADS + 1))
                for k in range(n):
                    if k == (n - 2 if s == 0 else 2):
                        dve.wait_ge(hi_ready, s + 1)
                        nc.vector.tensor_tensor(table_lo[:, s % 2, 0:n * D], table_raw[:, s % LOADS, 0:n * D],
                                                table_hi[:, s % 2, 0:n * D].bitcast(fp32),
                                                ALU.subtract).then_inc(lo_ready, 1)
                    c = before + k
                    if c >= SLOTS:
                        dve.wait_ge(one_hot_used, c - SLOTS + 1)
                    last = nc.vector.tensor_scalar(one_hot[:, c % SLOTS, :], ids_all[0:TROWS, s % LOADS, :],
                                                   row_of[n][:, k:k + 1], None, ALU.is_equal)
                    last.then_inc(one_hot_ready, 1)
                dve.wait_ge(one_hot_ready, before + n)
                dve.wait_ge(lo_ready, s + 1)
                dve.sem_inc(ids_all_used, 1)

            def layer1(t):
                if t == 0:
                    dve.wait_ge(weights_in, 96)
                dve.wait_ge(h1_summed, 2 * t + 1)
                for m in range(0, M1, 2):
                    nc.vector.tensor_scalar(h1_t[:, m, :], h1_ps[m], b1_sb[:, m:m + 1], 0.0,
                                            ALU.add, ALU.max).then_inc(h1_ready[0], 1)

            def layer2(t):
                dve.wait_ge(h2_summed, M2 * t + 1)
                nc.vector.tensor_scalar(h2_t[:, t, 0, :], h2_ps[0], b2_sb[:, 0:1], 0.0,
                                        ALU.add, ALU.max).then_inc(h2_ready[0], 1)

            def take_steps(t, q):
                for step, i in steps_after(t, q):
                    if step == "select" and i + 1 < NS:
                        make_one_hot(i + 1)
                    if step == "layer1":
                        layer1(i)
                    if step == "layer2":
                        layer2(i)

            dve.wait_ge(rows_numbered, len(row_int))
            for rows in row_int:
                last = nc.vector.tensor_copy(row_of[rows.shape[1]][:], rows[:])
                last.then_inc(row_of_ready, 1)
            dve.wait_ge(row_of_ready, len(row_int))
            make_one_hot(0)
            take_steps(0, "start")
            for t in range(TILES):
                for q in range(len(quads(t))):
                    take_steps(t, q)
                dve.wait_ge(gram_ready, t + 1)
                if t >= 1:
                    dve.wait_ge(packed_ready, t)
                by_j = gram_ps[:].rearrange("p g j -> p j g")
                to_j = pairs[:].rearrange("p (i j) -> p j i", j=PITCH)
                nc.vector.transpose(to_j[:, 1:NF, :], by_j[:, 1:NF, :])
                nc.vector.transpose(to_j[:, NF:PITCH, :], by_j[:, 0:SHIFTS, :]).then_inc(pairs_ready, 1)
                dve.wait_ge(pairs_ready, t + 1)
                if t >= 2:
                    dve.wait_ge(pairs_transposed, t - 1)
                rows = pairs[:, 1:1 + NF * (PITCH + 1)].rearrange("p (i s) -> p i s", i=NF)
                nc.vector.tensor_copy(packed[:, t % 2, :].rearrange("p (i s) -> p i s", i=NF),
                                      rows[:, :, 0:SHIFTS]).then_inc(packed_ready, 1)
                take_steps(t, "gram")

        @block.scalar
        def _(act):
            def round_table(s):
                act.wait_ge(table_in[s % LOADS], 32 * (s // LOADS + 1))
                if s >= 2:
                    act.wait_ge(ring_filled, turn["select", s - 2] + 1)
                nc.scalar.copy(table_hi[:, s % 2, 0:CHUNKS[s] * D],
                               table_raw[:, s % LOADS, 0:CHUNKS[s] * D]).then_inc(hi_ready, 1)

            def copy_selected(s):
                n = turn["select", s]
                act.wait_ge(ring_filled, n + 1)
                nc.scalar.copy(feat_v[:, TS:TILES, :, NF - NS + s],
                               ring[n % RING][:, 0:TILES - TS, :]).then_inc(ring_copied, 1)

            def copy_pairs(t):
                act.wait_ge(pairs_transposed, t + 1)
                nc.scalar.copy(pairs_t[:], pairs_t_ps[0:KI * SHIFTS, 0:KP, :]).then_inc(pairs_t_ready, 1)

            def layer1(t):
                if t == 0:
                    act.wait_ge(weights_in, 96)
                act.wait_ge(h1_summed, 2 * t + 2)
                for m in range(1, M1, 2):
                    nc.scalar.activation(h1_t[:, m, :], h1_ps[m], ACT.Relu,
                                         bias=b1_sb[:, m:m + 1]).then_inc(h1_ready[1], 1)

            def layer2(t):
                act.wait_ge(h2_summed, M2 * t + 2)
                nc.scalar.activation(h2_t[:, t, 1, :], h2_ps[1], ACT.Relu,
                                     bias=b2_sb[:, 1:2]).then_inc(h2_ready[1], 1)

            def layer3(t):
                n = turn["layer3", t]
                act.wait_ge(ring_filled, n + 1)
                nc.scalar.copy(y_row[:, t * P:(t + 1) * P], ring[n % RING][0:1, 0, :]).then_inc(ring_copied, 1)

            def take_steps(t, q):
                for step, i in steps_after(t, q):
                    if step == "select":
                        copy_selected(i)
                        if i + 2 < NS:
                            round_table(i + 2)
                    if step == "pairs":
                        copy_pairs(i)
                    if step == "layer1":
                        layer1(i)
                    if step == "layer2":
                        layer2(i)
                    if step == "layer3":
                        layer3(i)

            for s in range(min(2, NS)):
                round_table(s)
            take_steps(0, "start")
            for t in range(TILES):
                for q, features in enumerate(quads(t)):
                    n = turn["quad", t, q]
                    act.wait_ge(ring_filled, n + 1)
                    nc.scalar.copy(feat_v[:, t, :, features[0]:features[-1] + 1].rearrange("p b f -> p f b"),
                                   ring[n % RING][:, 0:len(features), :]).then_inc(ring_copied, 1)
                    take_steps(t, q)
                take_steps(t, "gram")

        @block.tensor
        def _(pe):
            def ring_free(n):
                if n >= RING:
                    pe.wait_ge(ring_copied, n - RING + 1)

            def select(s):
                n, before = turn["select", s], sum(CHUNKS[:s])
                ring_free(n)
                for k in range(CHUNKS[s]):
                    c = before + k
                    pe.wait_ge(one_hot_ready, c + 1)
                    if k == 0:
                        pe.wait_ge(hi_ready, s + 1)
                        pe.wait_ge(lo_ready, s + 1)
                    for part in (table_hi, table_lo):
                        last = nc.tensor.matmul(ring[n % RING][:, 0:TILES - TS, :],
                                                part[:, s % 2, k * D:(k + 1) * D], one_hot[:, c % SLOTS, :],
                                                start=(k == 0 and part is table_hi),
                                                stop=(k == CHUNKS[s] - 1 and part is table_lo))
                    last.then_inc(one_hot_used, 1)
                pe.wait_ge(one_hot_used, before + CHUNKS[s])
                pe.sem_inc(ring_filled, 1)

            def layer1_sum(m, weights, inputs, first=False, last=False):
                return nc.tensor.matmul(h1_ps[m], weights[:, m * P:(m + 1) * P], inputs,
                                        start=first and m < 2, stop=last, skip_group_check=True)

            BY_BANK = [*range(0, M1, 2), *range(1, M1, 2)]

            def transpose_pairs(t):
                pe.wait_ge(packed_ready, t + 1)
                if t >= 1:
                    pe.wait_ge(h2_ready[1], t)
                for k in range(KP):
                    last = nc.tensor.transpose(pairs_t_ps[0:KI * SHIFTS, k, :],
                                               packed[:, t % 2, KI * SHIFTS * k:KI * SHIFTS * (k + 1)],
                                               identity[:])
                last.then_inc(pairs_transposed, 1)

            def dense_part(t):
                if t == 0:
                    pe.wait_ge(weights_in, 96)
                for m in BY_BANK:
                    if t >= 1 and m < 2:
                        pe.wait_ge([h2_ready[0], h1_ready[1]][m], [t, (M1 // 2) * t][m])
                    layer1_sum(m, w1d_sb, feat_v[:, t, :, 0], first=True)

            def layer1(t):
                pe.wait_ge(pairs_t_ready, t + 1)
                for m in BY_BANK:
                    for k in range(KP):
                        last = layer1_sum(m, w1p_sb[:, k, :], pairs_t[:, k, :], last=(k == KP - 1))
                    if m >= M1 - 2:
                        last.then_inc(h1_summed, 1)

            def layer2(t):
                for half in range(2):
                    for m in range(M2):
                        for k in range(half, M1, 2):
                            if m == 0:
                                pe.wait_ge(h1_ready[half], (M1 // 2) * t + k // 2 + 1)
                            if m == 0 and k == 0:
                                pe.wait_ge(h1_ready[0], (M1 // 2) * (t + 1))
                            last = nc.tensor.matmul(h2_ps[m], w2_sb[:, k, m * P:(m + 1) * P], h1_t[:, k, :],
                                                    start=(k == 0), stop=(k == M1 - 1))
                        if half == 1:
                            last.then_inc(h2_summed, 1)

            def layer3(t):
                n = turn["layer3", t]
                ring_free(n)
                for k in range(M2):
                    pe.wait_ge(h2_ready[k], t + 1)
                    last = nc.tensor.matmul(ring[n % RING][0:1, 0, :], w3_sb[:, k:k + 1], h2_t[:, t, k, :],
                                            start=(k == 0), stop=(k == M2 - 1))
                last.then_inc(ring_filled, 1)

            def warm(count):
                n = turn["layer3", TILES - 2]
                ring_free(n)
                for _ in range(count):
                    nc.tensor.matmul(ring[n % RING][:, 0, :], identity[:], identity[:], start=True, stop=True)

            def take_steps(t, q):
                for step, i in steps_after(t, q):
                    {"select": select, "pairs": transpose_pairs, "dense": dense_part, "layer1": layer1,
                     "layer2": layer2, "layer3": layer3, "warm": warm}[step](i)

            take_steps(0, "start")
            pe.wait_ge(identity_ready, 1)
            pe.wait_ge(dense_in, 16)
            pe.wait_ge(tail_zero, 1)
            for t in range(TILES):
                for q, features in enumerate(quads(t)):
                    n = turn["quad", t, q]
                    pe.wait_ge(gathered[t][q], 16 * sum(1 for f in features if f > 0))
                    ring_free(n)
                    for k, f in enumerate(features):
                        rows = emb[t][:, f - 1, :] if f > 0 else dense_sb[:, t, :]
                        last = nc.tensor.transpose(ring[n % RING][:, k, :], rows, identity[:])
                    last.then_inc(ring_filled, 1)
                    take_steps(t, q)
                gathered_last = turn["quad", t, len(quads(t)) - 1]
                pe.wait_ge(ring_copied, 1 + (gathered_last if t < TS else max(gathered_last, turn.get(("select", NS - 1), 0))))
                if t >= 1:
                    pe.wait_ge(pairs_ready, t)
                for g in range(BLK):
                    for c in range(QUADRANTS):
                        at = (BLK * c + g) * NF
                        last = nc.tensor.matmul(gram_ps[BLK * c:BLK * (c + 1), g, 0:NF],
                                                feat_t[:, t, at:at + BLK], feat_t[:, t, at:at + NF],
                                                start=True, stop=True)
                last.then_inc(gram_ready, 1)
                take_steps(t, "gram")


_TABLES = 26
_FEATURES = _TABLES + 1
_P = 128
_SELECTED = (6, 7, 9, 14, 16, 17, 18, 1, 5)
_SELECTED_FROM = 1
_ORDER = tuple(f for f in range(_TABLES) if f not in _SELECTED) + _SELECTED


def _pair_rows():
    import numpy as _np

    row = {}
    for a in range(_FEATURES):
        for b in range(a + 1, _FEATURES):
            row[a, b] = len(row)
    feature = (0,) + tuple(f + 1 for f in _ORDER)
    rows = []
    for i in range(_FEATURES):
        for s in range(1, _FEATURES // 2 + 1):
            rows.append(row[tuple(sorted((feature[i], feature[(i + s) % _FEATURES])))])
    return _np.array(rows)


def kernel(**inputs):
    import numpy as _np
    import concourse.bacc as _bacc
    from concourse import mybir as _mybir
    from concourse.bass_utils import run_bass_kernel_spmd as _run

    ids = _np.asarray(inputs["ids"])[:, list(_ORDER)]
    w1 = _np.asarray(inputs["W_top1"])
    batch = ids.shape[0]
    rows = _pair_rows()
    laid_out = {
        "ids": ids.reshape(batch // _P, _P, _TABLES).transpose(1, 0, 2),
        "picked_ids": ids[_SELECTED_FROM * _P:, _TABLES - len(_SELECTED):].T,
        "dense": _np.asarray(inputs["r_dense_features"]),
        "w1_pairs": w1[rows].reshape(3, len(rows) // 3, -1).transpose(1, 0, 2),
        "w1_dense": w1[len(rows):],
        "b1": _np.asarray(inputs["b_top1"]).reshape(-1, _P).T,
        "w2": _np.asarray(inputs["W_top2"]),
        "b2": _np.asarray(inputs["b_top2"]).reshape(-1, _P).T,
        "w3": _np.asarray(inputs["W_top3"]).reshape(-1, _P).T,
    }
    for f in range(_TABLES):
        laid_out[f"tbl_{f}"] = _np.asarray(inputs[f"tbl_{f}"])

    nc = _bacc.Bacc("TRN2", target_bir_lowering=False, num_devices=1)
    arrays, aps = {}, {}
    for name, a in laid_out.items():
        a = _np.ascontiguousarray(a)
        arrays[f"in_{name}_dram"] = a
        aps[name] = nc.dram_tensor(f"in_{name}_dram", a.shape, _mybir.dt.from_np(a.dtype),
                                   kind="ExternalInput").ap()
    out = nc.dram_tensor("out_dram", (1, batch), _mybir.dt.float32, kind="ExternalOutput").ap()
    dlrm_tower(nc, aps["ids"], aps["picked_ids"], aps["dense"], [aps[f"tbl_{f}"] for f in _ORDER],
               aps["w1_pairs"], aps["w1_dense"], aps["b1"], aps["w2"], aps["b2"], aps["w3"], out)
    r = _run(nc, [arrays], core_ids=[0])
    return r.results[0]["out_dram"].reshape(batch, 1)
```

```python
import concourse.bass as bass
from concourse import mybir
from contextlib import ExitStack


def dlrm_tower(nc, ids, picked_ids, picked_from, dense, tables, w1_pairs, w1_dense, b1, w2, b2, w3, out):
    fp32 = mybir.dt.float32
    fp32r = mybir.dt.float32r
    int32 = mybir.dt.int32
    ALU = mybir.AluOpType
    ACT = mybir.ActivationFunctionType

    P = 128
    BATCH = out.shape[1]
    TILES = BATCH // P
    D = dense.shape[0]
    NT = len(tables)
    NF = NT + 1
    QUAD = 4
    NS = picked_ids.shape[0]
    picked_tables = tables[NT - NS:][::-1]
    TROWS = 125
    CHUNKS = [tbl.shape[0] // TROWS for tbl in picked_tables]
    KMAX = max(CHUNKS)
    LAST = [2 if n > 8 and first == 0 else 1 for n, first in zip(CHUNKS, picked_from)]
    MADE = [n - last for n, last in zip(CHUNKS, LAST)]
    HOTS = 3
    SLOTS = 13
    LOADS = 3
    PARTS = 3
    AHEAD = 2
    SHIFTS = NF // 2
    PAIRS = NF * (NF - 1) // 2
    KP = 3
    K = PAIRS // KP
    H1, H2 = w1_dense.shape[1], w2.shape[1]
    M1, M2 = H1 // P, H2 // P
    BLK = 32
    QUADRANTS = P // BLK

    def quads(t):
        n = NF - sum(1 for first in picked_from if first <= t)
        return [range(max(f, 1), min(f + QUAD, n)) for f in range(0, n, QUAD)]

    STEPS = {
        (0, "start"): [("select", 0)],
        (0, 0): [("select", 1), ("place", 0)],
        (0, 1): [("select", 2)],
        (0, 2): [("select", 3)],
        (0, 3): [("select", 4)],
        (0, 4): [("select", 5), ("select", 6), ("select", 7), ("quad", (1, 0)), ("quad", (1, 1))],
        (0, "gram"): [("select", 8)],
        (1, 1): [("pairs", 0), ("dense", 0)],
        (1, 3): [("layer1", 0)],
        (1, 4): [("layer2", 0)],
        (2, 3): [("layer3", 0), ("pairs", 1), ("dense", 1), ("layer1", 1)],
        (2, 4): [("layer2", 1)],
        (3, 2): [("layer3", 1), ("pairs", 2), ("dense", 2), ("layer1", 2)],
        (3, 4): [("warm", 2)],
        (3, "gram"): [("layer2", 2), ("pairs", 3), ("dense", 3), ("layer1", 3), ("layer2", 3), ("layer3", 2),
                      ("layer3", 3)],
    }

    def steps_after(t, q):
        return STEPS.get((t, q), [])

    RING = 3
    WARM_START = 11
    early = [i for after in STEPS.values() for step, i in after if step == "quad"]
    turn, warm_turn, turns = {}, {}, 0
    for t, q in [(0, "start")] + [(t, q) for t in range(TILES) for q in [*range(len(quads(t))), "gram"]]:
        taking = [step for step in steps_after(t, q) if step[0] in ("quad", "select", "layer2", "layer3", "warm")]
        if q in range(len(quads(t))) and (t, q) not in early:
            taking = [("quad", (t, q))] + taking
        for step in taking:
            if step[0] == "warm":
                warm_turn[t, q] = turns
            else:
                turn[step] = turns
                turns += 1

    ctx = ExitStack()
    with ctx:
        def sb(name, shape, dt=fp32):
            return ctx.enter_context(nc.sbuf_tensor(name, shape, dt))

        def ps(name, shape):
            return ctx.enter_context(nc.psum_tensor(name, shape, fp32))

        def sem(name):
            return ctx.enter_context(nc.semaphore(name))

        ids_sb = sb("ids_sb", [P, TILES, NT], int32)
        dense_t = sb("dense_t", [D, BATCH])
        emb = [sb(f"emb{t}", [P, quads(t)[-1][-1], D]) for t in range(TILES)]
        identity = sb("identity", [P, P])
        feat_t = sb("feat_t", [P, TILES, P * NF + BLK - NF])
        feat_v = feat_t[:, :, 0:P * NF].rearrange("p t (b f) -> p t b f", f=NF)
        pairs = sb("pairs", [P, BLK * NF])
        packed = sb("packed", [P, 2, PAIRS])
        pairs_t = sb("pairs_t", [K, KP, P])
        h1_t = sb("h1_t", [P, M1, P])
        h2_t = sb("h2_t", [P, TILES, M2, P])
        ids_all = sb("ids_all", [P, LOADS, BATCH], int32)
        row_int = [sb(f"row_int{k}", [TROWS, k], int32) for k in sorted(set(CHUNKS))]
        row_of = {k: sb(f"row_of{k}", [TROWS, k]) for k in sorted(set(CHUNKS))}
        table_raw = sb("table_raw", [TROWS, LOADS, KMAX * D])
        table_hi = sb("table_hi", [TROWS, PARTS, KMAX * D], fp32r)
        table_lo = sb("table_lo", [TROWS, PARTS, KMAX * D], fp32r)
        distance = sb("distance", [TROWS, 2, BATCH])
        last_hot = sb("last_hot", [TROWS, HOTS, BATCH], fp32r)
        one_hot = sb("one_hot", [TROWS, SLOTS, BATCH], fp32r)
        unread = sb("unread", [TROWS, 1])
        y_row = sb("y_row", [1, BATCH])
        w1p_sb = sb("w1p_sb", [K, KP, H1])
        w1d_sb = sb("w1d_sb", [P, H1])
        w2_sb = sb("w2_sb", [P, M1, H2])
        w3_sb = sb("w3_sb", [P, M2])
        b1_sb = sb("b1_sb", [P, M1])
        b2_sb = sb("b2_sb", [P, M2])

        ring = [ps(f"ring{i}", [P, QUAD, P]) for i in range(RING)]
        gram_ps = ps("gram_ps", [P, BLK, BLK])
        pairs_t_ps = ps("pairs_t_ps", [K, KP, P])
        mlp_ps = [ps(f"mlp_ps{i}", [P, QUAD, P]) for i in range(2)]
        h1_ps = [mlp_ps[m % 2][:, m // 2, :] for m in range(M1)]
        h2_ps = mlp_ps[0][:, M1 // 2, :]

        ids_in = sem("ids_in")
        dense_in = sem("dense_in")
        dense_placed = sem("dense_placed")
        weights_in = sem("weights_in")
        identity_zero = sem("identity_zero")
        identity_ready = sem("identity_ready")
        tail_zero = sem("tail_zero")
        gathered = [[sem(f"gathered_{t}_{q}") for q in range(len(quads(t)))] for t in range(TILES)]
        ring_filled = sem("ring_filled")
        ring_copied = sem("ring_copied")
        rows_numbered = sem("rows_numbered")
        row_of_ready = sem("row_of_ready")
        ids_all_in = [sem(f"ids_all_in{i}") for i in range(LOADS)]
        table_in = [sem(f"table_in{i}") for i in range(LOADS)]
        hi_ready = sem("hi_ready")
        lo_ready = sem("lo_ready")
        one_hot_ready = sem("one_hot_ready")
        one_hot_used = sem("one_hot_used")
        distance_ready = sem("distance_ready")
        last_hot_ready = sem("last_hot_ready")
        gram_ready = sem("gram_ready")
        pairs_ready = sem("pairs_ready")
        packed_ready = sem("packed_ready")
        pairs_transposed = sem("pairs_transposed")
        pairs_t_ready = sem("pairs_t_ready")
        h1_summed = sem("h1_summed")
        h1_ready = [sem("h1_ready_dve"), sem("h1_ready_act")]
        h2_summed = sem("h2_summed")
        h2_ready = sem("h2_ready")
        y_out = sem("y_out")

        block = ctx.enter_context(nc.Block())

        @block.sync
        def _(sp):
            sp.dma_start(ids_sb[:], ids).then_inc(ids_in, 16)

            def load_table(s):
                if s >= LOADS:
                    sp.wait_ge(one_hot_ready, sum(MADE[:s - LOADS + 1]))
                    sp.wait_ge(lo_ready, s - LOADS + 1)
                    sp.wait_ge(last_hot_ready, sum(LAST[:s - LOADS + 1]))
                sp.dma_start(ids_all[:, s % LOADS, :],
                             picked_ids[s:s + 1, :].to_broadcast([P, BATCH])).then_inc(
                                 ids_all_in[s % LOADS], 16)
                n = CHUNKS[s]
                rows = picked_tables[s].rearrange("(p k) d -> p (k d)", k=n)
                for a, b in ((0, 112), (112, TROWS)):
                    sp.dma_start(table_raw[a:b, s % LOADS, 0:n * D], rows[a:b, :]).then_inc(
                        table_in[s % LOADS], 16)

            load_table(0)
            sp.dma_start(dense_t[:], dense).then_inc(dense_in, 16)
            for s in range(1, NS):
                load_table(s)
            for dst, src in ((w1p_sb[:], w1_pairs), (w1d_sb[:], w1_dense),
                             (w2_sb[:], w2.rearrange("(k p) n -> p k n", p=P)),
                             (b1_sb[:], b1), (b2_sb[:], b2), (w3_sb[:], w3)):
                sp.dma_start(dst, src).then_inc(weights_in, 16)
            sp.wait_ge(ring_copied, turns)
            sp.dma_start(out, y_row[:]).then_inc(y_out, 16)
            sp.wait_ge(y_out, 16)

        @block.gpsimd
        def _(pool):
            nc.gpsimd.memset(feat_t[:, :, P * NF:], 0.0).then_inc(tail_zero, 1)
            nc.gpsimd.memset(identity[:], 0.0).then_inc(identity_zero, 1)
            for rows in row_int:
                nc.gpsimd.iota(rows[:], pattern=[[1, rows.shape[1]]], base=0,
                               channel_multiplier=rows.shape[1]).then_inc(rows_numbered, 1)
            pool.wait_ge(identity_zero, 1)
            nc.gpsimd.affine_select(out=identity[:], in_=identity[:], compare_op=ALU.not_equal, fill=1.0,
                                    base=0, pattern=[[-1, P]], channel_multiplier=1).then_inc(identity_ready, 1)
            pool.wait_ge(ids_in, 16)
            for t in range(TILES):
                for q, features in enumerate(quads(t)):
                    for f in features:
                        pool.indirect_dma_start(
                            emb[t][:, f - 1, :], None, tables[f - 1],
                            bass.IndirectOffsetOnAxis(ap=ids_sb[:, t, f - 1:f], axis=0),
                        ).then_inc(gathered[t][q], 16)

        @block.vector
        def _(dve):
            def make_one_hot(s):
                n, before = CHUNKS[s], sum(MADE[:s])
                start = picked_from[s] * P
                dve.wait_ge(ids_all_in[s % LOADS], 16 * (s // LOADS + 1))
                for k in range(MADE[s]):
                    c = before + k
                    if c >= SLOTS:
                        dve.wait_ge(one_hot_used, c - SLOTS + 1)
                    last = nc.vector.tensor_scalar(one_hot[:, c % SLOTS, start:], ids_all[0:TROWS, s % LOADS, start:],
                                                   row_of[n][:, k:k + 1], None, ALU.is_equal)
                    last.then_inc(one_hot_ready, 1)
                dve.wait_ge(hi_ready, s + 1)
                if s >= PARTS:
                    dve.wait_ge(ring_filled, turn["select", s - PARTS] + 1)
                nc.vector.tensor_tensor(table_lo[:, s % PARTS, 0:n * D], table_raw[:, s % LOADS, 0:n * D],
                                        table_hi[:, s % PARTS, 0:n * D].bitcast(fp32),
                                        ALU.subtract).then_inc(lo_ready, 1)

            def layer1(t):
                if t == 0:
                    dve.wait_ge(weights_in, 96)
                dve.wait_ge(h1_summed, 2 * t + 1)
                for m in range(0, M1, 2):
                    nc.vector.tensor_scalar(h1_t[:, m, :], h1_ps[m], b1_sb[:, m:m + 1], 0.0,
                                            ALU.add, ALU.max).then_inc(h1_ready[0], 1)

            def layer2(t):
                dve.wait_ge(h2_summed, t + 1)
                nc.vector.tensor_scalar(h2_t[:, t, 0, :], h2_ps, b2_sb[:, 0:1], 0.0,
                                        ALU.add, ALU.max).then_inc(h2_ready, 1)

            def take_steps(t, q):
                for step, i in steps_after(t, q):
                    if step == "select" and i + 1 < NS:
                        make_one_hot(i + 1)
                    if step == "layer1":
                        layer1(i)
                    if step == "layer2":
                        layer2(i)

            dve.wait_ge(rows_numbered, len(row_int))
            for rows in row_int:
                last = nc.vector.tensor_copy(row_of[rows.shape[1]][:], rows[:])
                last.then_inc(row_of_ready, 1)
            dve.wait_ge(row_of_ready, len(row_int))
            make_one_hot(0)
            take_steps(0, "start")
            for t in range(TILES):
                for q in range(len(quads(t))):
                    take_steps(t, q)
                dve.wait_ge(gram_ready, t + 1)
                if t >= 1:
                    dve.wait_ge(packed_ready, 2 * t)
                nc.vector.transpose(pairs[:].rearrange("p (i j) -> p j i", j=NF),
                                    gram_ps[:, :, 0:NF].rearrange("p g j -> p j g")).then_inc(pairs_ready, 1)
                dve.wait_ge(pairs_ready, t + 1)
                if t >= 2:
                    dve.wait_ge(pairs_transposed, t - 1)
                rows = pairs[:, 0:(NF - 1) * (NF + 1)].rearrange("p (i s) -> p i s", i=NF - 1)
                most = (NF - 1) * SHIFTS
                nc.vector.tensor_copy(packed[:, t % 2, 0:most].rearrange("p (i s) -> p i s", i=NF - 1),
                                      rows[:, :, 1:SHIFTS + 1]).then_inc(packed_ready, 1)
                nc.vector.tensor_copy(packed[:, t % 2, most:PAIRS],
                                      rows[:, 0:SHIFTS, SHIFTS + 1]).then_inc(packed_ready, 1)
                take_steps(t, "gram")

        @block.scalar
        def _(act):
            def round_table(s):
                act.wait_ge(table_in[s % LOADS], 32 * (s // LOADS + 1))
                if s >= PARTS:
                    act.wait_ge(ring_filled, turn["select", s - PARTS] + 1)
                nc.scalar.copy(table_hi[:, s % PARTS, 0:CHUNKS[s] * D],
                               table_raw[:, s % LOADS, 0:CHUNKS[s] * D]).then_inc(hi_ready, 1)

            def make_last_hot(s):
                start = picked_from[s] * P
                act.wait_ge(ids_all_in[s % LOADS], 16 * (s // LOADS + 1))
                for k in range(MADE[s], CHUNKS[s]):
                    h = sum(LAST[:s]) + k - MADE[s]
                    if h >= 2:
                        act.wait_ge(last_hot_ready, h - 1)
                    nc.scalar.activation(distance[:, h % 2, start:], ids_all[0:TROWS, s % LOADS, start:], ACT.Square,
                                         bias=row_of[CHUNKS[s]][:, k:k + 1], scale=-1.0).then_inc(distance_ready, 1)
                    act.wait_ge(distance_ready, h + 1)
                    nc.scalar.activation(last_hot[:, h % HOTS, start:], distance[:, h % 2, start:], ACT.Relu,
                                         bias=1.0, scale=-1.0).then_inc(last_hot_ready, 1)

            def copy_quad(t, q):
                n, features = turn["quad", (t, q)], quads(t)[q]
                act.wait_ge(ring_filled, n + 1)
                nc.scalar.copy(feat_v[:, t, :, features[0]:features[-1] + 1].rearrange("p b f -> p f b"),
                               ring[n % RING][:, 0:len(features), :]).then_inc(ring_copied, 1)

            def copy_selected(s):
                n = turn["select", s]
                act.wait_ge(ring_filled, n + 1)
                first = picked_from[s]
                nc.scalar.copy(feat_v[:, first:, :, NF - 1 - s],
                               ring[n % RING][:, first:TILES, :]).then_inc(ring_copied, 1)

            def copy_pairs(t):
                act.wait_ge(pairs_transposed, t + 1)
                nc.scalar.copy(pairs_t[:], pairs_t_ps[:]).then_inc(pairs_t_ready, 1)

            def layer1(t):
                if t == 0:
                    act.wait_ge(weights_in, 96)
                act.wait_ge(h1_summed, 2 * t + 2)
                for m in range(1, M1, 2):
                    nc.scalar.activation(h1_t[:, m, :], h1_ps[m], ACT.Relu,
                                         bias=b1_sb[:, m:m + 1]).then_inc(h1_ready[1], 1)

            def layer2(t):
                n = turn["layer2", t]
                act.wait_ge(ring_filled, n + 1)
                nc.scalar.activation(h2_t[:, t, 1, :], ring[n % RING][:, 0, :], ACT.Relu,
                                     bias=b2_sb[:, 1:2]).then_inc(ring_copied, 1)

            def layer3(t):
                n = turn["layer3", t]
                act.wait_ge(ring_filled, n + 1)
                nc.scalar.copy(y_row[:, t * P:(t + 1) * P], ring[n % RING][0:1, 0, :]).then_inc(ring_copied, 1)

            def take_steps(t, q):
                for step, i in steps_after(t, q):
                    if step == "select":
                        if i + 1 < NS:
                            make_last_hot(i + 1)
                        copy_selected(i)
                        if i + AHEAD < NS:
                            round_table(i + AHEAD)
                    if step == "quad":
                        copy_quad(*i)
                    if step == "place":
                        act.wait_ge(dense_in, 16)
                        nc.scalar.copy(feat_v[:, :, :, 0],
                                       dense_t[:].rearrange("d (t b) -> d t b", b=P)).then_inc(dense_placed, 1)
                    if step == "pairs":
                        copy_pairs(i)
                    if step == "layer1":
                        layer1(i)
                    if step == "layer2":
                        layer2(i)
                    if step == "layer3":
                        layer3(i)

            act.wait_ge(row_of_ready, len(row_int))
            nc.scalar.activation(unread[:], row_of[CHUNKS[0]][:, 0:1], ACT.Square)
            make_last_hot(0)
            for s in range(min(AHEAD, NS)):
                round_table(s)
            take_steps(0, "start")
            for t in range(TILES):
                for q in range(len(quads(t))):
                    if (t, q) not in early:
                        copy_quad(t, q)
                    take_steps(t, q)
                take_steps(t, "gram")

        @block.tensor
        def _(pe):
            def ring_free(n):
                if n >= RING:
                    pe.wait_ge(ring_copied, n - RING + 1)

            def transpose_quad(tile_and_quad):
                t, q = tile_and_quad
                n, features = turn["quad", (t, q)], quads(t)[q]
                pe.wait_ge(gathered[t][q], 16 * len(features))
                ring_free(n)
                for k, f in enumerate(features):
                    last = nc.tensor.transpose(ring[n % RING][:, k, :], emb[t][:, f - 1, :], identity[:])
                last.then_inc(ring_filled, 1)

            def select(s):
                n, before, first = turn["select", s], sum(MADE[:s]), picked_from[s]
                ring_free(n)
                pe.wait_ge(hi_ready, s + 1)
                for part in (table_hi, table_lo):
                    if part is table_lo:
                        pe.wait_ge(lo_ready, s + 1)
                    for k in range(CHUNKS[s]):
                        c = before + k
                        if k < MADE[s]:
                            if part is table_hi:
                                pe.wait_ge(one_hot_ready, c + 1)
                            rows = one_hot[:, c % SLOTS, first * P:]
                        else:
                            h = sum(LAST[:s]) + k - MADE[s]
                            if part is table_hi:
                                pe.wait_ge(last_hot_ready, h + 1)
                            rows = last_hot[:, h % HOTS, first * P:]
                        last = nc.tensor.matmul(ring[n % RING][:, first:TILES, :],
                                                part[:, s % PARTS, k * D:(k + 1) * D], rows,
                                                start=(k == 0 and part is table_hi),
                                                stop=(k == CHUNKS[s] - 1 and part is table_lo))
                        if part is table_lo:
                            if k < MADE[s]:
                                last.then_inc(one_hot_used, 1)
                            elif k == CHUNKS[s] - 1:
                                last.then_inc(ring_filled, 1)

            def layer1_sum(m, weights, inputs, first=False, last=False):
                return nc.tensor.matmul(h1_ps[m], weights[:, m * P:(m + 1) * P], inputs,
                                        start=first and m < 2, stop=last, skip_group_check=True)

            BY_BANK = [*range(0, M1, 2), *range(1, M1, 2)]

            def transpose_pairs(t):
                pe.wait_ge(packed_ready, 2 * (t + 1))
                if t >= 1:
                    pe.wait_ge(pairs_t_ready, t)
                for k in range(KP):
                    last = nc.tensor.transpose(pairs_t_ps[:, k, :],
                                               packed[:, t % 2, K * k:K * (k + 1)],
                                               identity[:])
                last.then_inc(pairs_transposed, 1)

            def dense_part(t):
                if t == 0:
                    pe.wait_ge(dense_in, 16)
                    pe.wait_ge(weights_in, 96)
                for m in BY_BANK:
                    if t >= 1 and m < 2:
                        pe.wait_ge([h2_ready, h1_ready[1]][m], [t, (M1 // 2) * t][m])
                    layer1_sum(m, w1d_sb, dense_t[:, t * P:(t + 1) * P], first=True)

            def layer1(t):
                pe.wait_ge(pairs_t_ready, t + 1)
                for m in BY_BANK:
                    for k in range(KP):
                        last = layer1_sum(m, w1p_sb[:, k, :], pairs_t[:, k, :], last=(k == KP - 1))
                    if m >= M1 - 2:
                        last.then_inc(h1_summed, 1)

            def layer2(t):
                n = turn["layer2", t]
                for half in range(2):
                    for m in range(M2):
                        for k in range(half, M1, 2):
                            if m == 0:
                                pe.wait_ge(h1_ready[half], (M1 // 2) * t + k // 2 + 1)
                            if m == 0 and k == 0:
                                pe.wait_ge(h1_ready[0], (M1 // 2) * (t + 1))
                            if m == 1 and k == 0:
                                ring_free(n)
                            last = nc.tensor.matmul([h2_ps, ring[n % RING][:, 0, :]][m],
                                                    w2_sb[:, k, m * P:(m + 1) * P], h1_t[:, k, :],
                                                    start=(k == 0), stop=(k == M1 - 1))
                        if half == 1:
                            last.then_inc([h2_summed, ring_filled][m], 1)

            def layer3(t):
                n = turn["layer3", t]
                ring_free(n)
                for k in range(M2):
                    pe.wait_ge([h2_ready, ring_copied][k], [t + 1, turn["layer2", t] + 1][k])
                    last = nc.tensor.matmul(ring[n % RING][0:1, 0, :], w3_sb[:, k:k + 1], h2_t[:, t, k, :],
                                            start=(k == 0), stop=(k == M2 - 1))
                last.then_inc(ring_filled, 1)

            def warm(count, n):
                ring_free(n)
                for _ in range(count):
                    nc.tensor.matmul(ring[n % RING][:, 0, :], identity[:], identity[:], start=True, stop=True)

            def take_steps(t, q):
                for step, i in steps_after(t, q):
                    if step == "warm":
                        warm(i, warm_turn[t, q])
                    elif step != "place":
                        {"quad": transpose_quad, "select": select, "pairs": transpose_pairs, "dense": dense_part,
                         "layer1": layer1, "layer2": layer2, "layer3": layer3}[step](i)

            pe.wait_ge(identity_ready, 1)
            warm(WARM_START, 0)
            take_steps(0, "start")
            pe.wait_ge(tail_zero, 1)
            for t in range(TILES):
                for q in range(len(quads(t))):
                    if (t, q) not in early:
                        transpose_quad((t, q))
                    take_steps(t, q)
                pe.wait_ge(dense_placed, 1)
                selected = [turn["select", s] for s in range(NS) if picked_from[s] <= t]
                pe.wait_ge(ring_copied, 1 + max(selected + [turn["quad", (t, len(quads(t)) - 1)]]))
                if t >= 1:
                    pe.wait_ge(pairs_ready, t)
                for g in range(BLK):
                    for c in range(QUADRANTS):
                        at = (BLK * c + g) * NF
                        last = nc.tensor.matmul(gram_ps[BLK * c:BLK * (c + 1), g, :],
                                                feat_t[:, t, at:at + BLK], feat_t[:, t, at:at + BLK],
                                                start=True, stop=True)
                last.then_inc(gram_ready, 1)
                take_steps(t, "gram")


_TABLES = 26
_FEATURES = _TABLES + 1
_P = 128
_SELECTED = (6, 7, 9, 14, 16, 17, 18, 1, 5)
_SELECTED_FROM = (0, 0, 0, 0, 0, 0, 0, 0, 1)
_ORDER = tuple(f for f in range(_TABLES) if f not in _SELECTED) + _SELECTED[::-1]


def _pair_rows():
    import numpy as _np

    row = {}
    for a in range(_FEATURES):
        for b in range(a + 1, _FEATURES):
            row[a, b] = len(row)
    feature = (0,) + tuple(f + 1 for f in _ORDER)
    shifts = _FEATURES // 2
    places = [(_FEATURES + 1) * i + s for i in range(_FEATURES - 1) for s in range(1, shifts + 1)]
    places += [(_FEATURES + 1) * i + shifts + 1 for i in range(shifts)]
    return _np.array([row[tuple(sorted((feature[p // _FEATURES], feature[p % _FEATURES])))] for p in places])


def kernel(**inputs):
    import numpy as _np
    import concourse.bacc as _bacc
    from concourse import mybir as _mybir
    from concourse.bass_utils import run_bass_kernel_spmd as _run

    ids = _np.asarray(inputs["ids"])[:, list(_ORDER)]
    w1 = _np.asarray(inputs["W_top1"])
    batch = ids.shape[0]
    rows = _pair_rows()
    laid_out = {
        "ids": ids.reshape(batch // _P, _P, _TABLES).transpose(1, 0, 2),
        "picked_ids": ids[:, _TABLES - len(_SELECTED):].T[::-1],
        "dense": _np.asarray(inputs["r_dense_features"]).T,
        "w1_pairs": w1[rows].reshape(3, len(rows) // 3, -1).transpose(1, 0, 2),
        "w1_dense": w1[len(rows):],
        "b1": _np.asarray(inputs["b_top1"]).reshape(-1, _P).T,
        "w2": _np.asarray(inputs["W_top2"]),
        "b2": _np.asarray(inputs["b_top2"]).reshape(-1, _P).T,
        "w3": _np.asarray(inputs["W_top3"]).reshape(-1, _P).T,
    }
    for f in range(_TABLES):
        laid_out[f"tbl_{f}"] = _np.asarray(inputs[f"tbl_{f}"])

    nc = _bacc.Bacc("TRN2", target_bir_lowering=False, num_devices=1)
    arrays, aps = {}, {}
    for name, a in laid_out.items():
        a = _np.ascontiguousarray(a)
        arrays[f"in_{name}_dram"] = a
        aps[name] = nc.dram_tensor(f"in_{name}_dram", a.shape, _mybir.dt.from_np(a.dtype),
                                   kind="ExternalInput").ap()
    out = nc.dram_tensor("out_dram", (1, batch), _mybir.dt.float32, kind="ExternalOutput").ap()
    dlrm_tower(nc, aps["ids"], aps["picked_ids"], _SELECTED_FROM, aps["dense"], [aps[f"tbl_{f}"] for f in _ORDER],
               aps["w1_pairs"], aps["w1_dense"], aps["b1"], aps["w2"], aps["b2"], aps["w3"], out)
    r = _run(nc, [arrays], core_ids=[0])
    return r.results[0]["out_dram"].reshape(batch, 1)
```
